# Optimizing a Trainium2 kernel written in Bass

```python
import numpy as np
import jax
import jax.numpy as jnp

def _softmax(x, axis=-1):
    return jax.nn.softmax(x, axis=axis)

def _gelu(x):
    return jax.nn.gelu(x, approximate=True)

def _silu(x):
    return jax.nn.silu(x)

def _sigmoid(x):
    return jax.nn.sigmoid(x)

def _layernorm(x, axis=-1, eps=1e-05):
    m = jnp.mean(x, axis=axis, keepdims=True)
    v = jnp.var(x, axis=axis, keepdims=True)
    return (x - m) / jnp.sqrt(v + eps)

def _scatter_add(tgt, idx, src, axis=0):
    return tgt.at[idx].add(src)

def _segment_sum(src, seg, n):
    return jax.ops.segment_sum(src, seg, n)
kernel_name = 'mk_adj_resnorm_d4_adj_r2_8e6857'

def setup_inputs(seed: int=0):
    np.random.seed(seed)
    _w = jnp.asarray

    def _rec_inputs():
        import jax
        import jax.numpy as jnp
        _gk = jax.random.key(seed)
        x = -0.000929 + 1 * jax.random.normal(jax.random.fold_in(_gk, 1), (8192, 128), jnp.float32)
        _w = (1.0 + jnp.arange(8192, dtype=jnp.float32)) ** (-0.5)
        _w = _w / _w.mean()
        _pij = jnp.clip(0.000244141 * _w[:, None] * _w[None, :], 0.0, 1.0)
        _a = jax.random.uniform(jax.random.fold_in(_gk, 2), (8192, 8192)) < _pij
        adj = _a.astype(jnp.int32)
        return (x, adj)
    x, adj = _rec_inputs()

    def _L0_gnn_setup():
        import jax, jax.numpy as jnp
        import numpy as np
        NEG_INF = -9000000000000000.0
        LEAKY_SLOPE = 0.01
        key = jax.random.key(seed)
        k1, k2, k3, k4 = jax.random.split(key, 4)
        N, F = (4096, 128)
        inp = jax.random.normal(k1, (N, F), dtype=jnp.float32)
        adj = jax.random.randint(k2, (N, N), 0, 2, dtype=jnp.int32)
        gain = 1.414
        limW = gain * np.sqrt(6.0 / (F + F))
        W = jax.random.uniform(k3, (F, F), minval=-limW, maxval=limW, dtype=jnp.float32)
        lima = gain * np.sqrt(6.0 / (2 * F + 1))
        a = jax.random.uniform(k4, (2 * F, 1), minval=-lima, maxval=lima, dtype=jnp.float32)
        return {'input': inp, 'adj': adj, 'W': W, 'a': a}
    _L0_gnn_all = _L0_gnn_setup()
    _L0_gnn_in = {k: v for k, v in _L0_gnn_all.items() if k in ('W', 'a')}
    del _L0_gnn_all

    def _L1_gnn_setup():
        import jax, jax.numpy as jnp
        import numpy as np
        N = 4096
        D_IN = 128
        D_OUT = 128
        ALPHA = 0.2
        NEG = -9000000000000000.0
        key = jax.random.key(seed)
        k1, k2, k3, k4 = jax.random.split(key, 4)
        input = jax.random.normal(k1, (N, D_IN), dtype=jnp.float32)
        adj = jax.random.randint(k2, (N, N), 0, 2, dtype=jnp.int32)
        lim_w = 1.414 * np.sqrt(6.0 / (D_IN + D_OUT))
        W = jax.random.uniform(k3, (D_IN, D_OUT), jnp.float32, -lim_w, lim_w)
        lim_a = 1.414 * np.sqrt(6.0 / (2 * D_OUT + 1))
        a = jax.random.uniform(k4, (2 * D_OUT, 1), jnp.float32, -lim_a, lim_a)
        return {'input': input, 'adj': adj, 'W': W, 'a': a}
    _L1_gnn_all = _L1_gnn_setup()
    _L1_gnn_in = {k: v for k, v in _L1_gnn_all.items() if k in ('W', 'a')}
    del _L1_gnn_all

    def _L2_gnn_setup():
        import jax, jax.numpy as jnp
        import numpy as np
        N = 4096
        IN_F = 128
        OUT_F = 128
        ALPHA = 0.2
        NEG_FILL = -9000000000000000.0
        key = jax.random.key(seed)
        k_adj, k_h, k_w, k_a = jax.random.split(key, 4)
        adj = jax.random.randint(k_adj, (N, N), 0, 2, dtype=jnp.int32)
        h = jax.random.normal(k_h, (N, IN_F), dtype=jnp.float32)
        W = jax.random.normal(k_w, (IN_F, OUT_F), dtype=jnp.float32) * (2.0 / (IN_F + OUT_F)) ** 0.5
        a = jax.random.normal(k_a, (2 * OUT_F, 1), dtype=jnp.float32) * (2.0 / (2 * OUT_F + 1)) ** 0.5
        return {'adj': adj, 'h': h, 'W': W, 'a': a}
    _L2_gnn_all = _L2_gnn_setup()
    _L2_gnn_in = {k: v for k, v in _L2_gnn_all.items() if k in ('W', 'a')}
    del _L2_gnn_all

    def _L3_gnn_setup():
        import jax, jax.numpy as jnp
        import numpy as np
        N = 6144
        IN_DIM = 128
        OUT_DIM = 128
        LR_SLOPE = 0.01
        NEG_INF = -9e+16
        key = jax.random.key(seed)
        k1, k2, k3, k4 = jax.random.split(key, 4)
        emb_mat = jax.random.normal(k1, (N, IN_DIM), dtype=jnp.float32)
        adj_mat = jax.random.randint(k2, (N, N), 0, 2, dtype=jnp.int32)
        W = jax.random.normal(k3, (OUT_DIM, IN_DIM), dtype=jnp.float32) * (2.0 / (IN_DIM + OUT_DIM)) ** 0.5
        a = jax.random.normal(k4, (2 * OUT_DIM, 1), dtype=jnp.float32) * (2.0 / (2 * OUT_DIM + 1)) ** 0.5
        return {'emb_mat': emb_mat, 'adj_mat': adj_mat, 'W': W, 'a': a}
    _L3_gnn_all = _L3_gnn_setup()
    _L3_gnn_in = {k: v for k, v in _L3_gnn_all.items() if k in ('W', 'a')}
    del _L3_gnn_all
    return {'x': x, 'adj': adj, 'L0_gnn_W': _L0_gnn_in['W'], 'L0_gnn_a': _L0_gnn_in['a'], 'L1_gnn_W': _L1_gnn_in['W'], 'L1_gnn_a': _L1_gnn_in['a'], 'L2_gnn_W': _L2_gnn_in['W'], 'L2_gnn_a': _L2_gnn_in['a'], 'L3_gnn_W': _L3_gnn_in['W'], 'L3_gnn_a': _L3_gnn_in['a']}

def reference(x, adj, L0_gnn_W, L0_gnn_a, L1_gnn_W, L1_gnn_a, L2_gnn_W, L2_gnn_a, L3_gnn_W, L3_gnn_a):
    import jax
    import jax.numpy as jnp

    def _L0_gnn_ref(input, adj, W, a):
        import jax, jax.numpy as jnp
        import numpy as np
        NEG_INF = -9000000000000000.0
        LEAKY_SLOPE = 0.01
        F_ = W.shape[0]
        h = input @ W
        a1, a2 = (a[:F_, 0], a[F_:, 0])
        s1 = h @ a1
        s2 = h @ a2
        e = jax.nn.leaky_relu(s1[:, None] + s2[None, :], negative_slope=LEAKY_SLOPE)
        masked = jnp.where(adj > 0, e, jnp.float32(NEG_INF))
        attention = jax.nn.softmax(masked, axis=1)
        return attention @ h

    def _L1_gnn_ref(input, adj, W, a):
        import jax, jax.numpy as jnp
        import numpy as np
        N = 4096
        D_IN = 128
        D_OUT = 128
        ALPHA = 0.2
        NEG = -9000000000000000.0
        h = input @ W
        a1 = a[:D_OUT, 0]
        a2 = a[D_OUT:, 0]
        e = (h @ a1)[:, None] + (h @ a2)[None, :]
        e = jnp.where(e > 0, e, ALPHA * e)
        e = jnp.where(adj > 0, e, NEG)
        attention = jax.nn.softmax(e, axis=1)
        h_prime = attention @ h
        return jax.nn.elu(h_prime)

    def _L2_gnn_ref(adj, h, W, a):
        import jax, jax.numpy as jnp
        import numpy as np
        N = 4096
        IN_F = 128
        OUT_F = 128
        ALPHA = 0.2
        NEG_FILL = -9000000000000000.0
        Wh = h @ W
        Wh1 = Wh @ a[:OUT_F, :]
        Wh2 = Wh @ a[OUT_F:, :]
        e = jax.nn.leaky_relu(Wh1 + Wh2.T, ALPHA)
        attention = jnp.where(adj > 0, e, jnp.float32(NEG_FILL))
        attention = jax.nn.softmax(attention, axis=1)
        h_prime = attention @ Wh
        return jax.nn.elu(h_prime)

    def _L3_gnn_ref(emb_mat, adj_mat, W, a):
        import jax, jax.numpy as jnp
        import numpy as np
        N = 6144
        IN_DIM = 128
        OUT_DIM = 128
        LR_SLOPE = 0.01
        NEG_INF = -9e+16
        out_dim = W.shape[0]
        e_new = emb_mat @ W.T
        a1 = a[:out_dim, :]
        a2 = a[out_dim:, :]
        source_scores = e_new @ a1
        target_scores = e_new @ a2
        e = source_scores + target_scores.T
        e = jax.nn.leaky_relu(e, negative_slope=LR_SLOPE)
        e = jnp.where(adj_mat > 0, e, NEG_INF)
        attention = jax.nn.softmax(e, axis=-1)
        e_transf = attention @ e_new
        return jax.nn.relu(e_transf)
    x = _layernorm(x + _L0_gnn_ref(x, adj, L0_gnn_W, L0_gnn_a), axis=-1)
    x = _layernorm(x + _L1_gnn_ref(x, adj, L1_gnn_W, L1_gnn_a), axis=-1)
    x = _layernorm(x + _L2_gnn_ref(adj, x, L2_gnn_W, L2_gnn_a), axis=-1)
    x = _layernorm(x + _L3_gnn_ref(x, adj, L3_gnn_W, L3_gnn_a), axis=-1)
    return x

_drawn_inputs = setup_inputs


def setup_inputs(seed=0):
    import zlib

    import numpy as np

    out = dict(_drawn_inputs(seed))
    spreads = {}
    factors = {}
    for name, (base, spread) in spreads.items():
        noise = np.random.default_rng([zlib.crc32(name.encode()), seed]).standard_normal(out[name].shape)
        drawn = base * np.exp(spread * noise) if base else spread * noise
        out[name] = jnp.asarray(drawn.astype(out[name].dtype))
    for name, factor in factors.items():
        out[name] = (out[name] * factor).astype(out[name].dtype)
    return out
```

```python
from contextlib import ExitStack

import concourse.bass as bass
from concourse import mybir

P = 128
ALU = mybir.AluOpType
ACT = mybir.ActivationFunctionType
AX = mybir.AxisListType
F32 = mybir.dt.float32
BF16 = mybir.dt.bfloat16
I32 = mybir.dt.int32
U32 = mybir.dt.uint32
U16 = mybir.dt.uint16

CAP = 16
QUARTERS = 4
SLOT_GROUPS = [(0, 1), (1, 1), (2, 1), (3, 1), (4, 1), (5, 1), (6, 2), (8, 4), (12, 4)]
BIG = 1e30
KEY0 = 0x2000
EPS = 1e-5
SLOPES = [0.01, 0.2, 0.2, 0.01]
ELU, RELU, NONE = "elu", "relu", "none"
AFTER = [NONE, ELU, ELU, RELU]
DENSE_MARK = 1000.0


def gat_layers(nc, x_in, adj_in, w_agg_in, w_score_in, a_in, out):
    N, F = x_in.shape
    T = N // P
    CB = T // QUARTERS
    QW = CB * P
    L = len(SLOPES)
    XC = F + 3
    TC = F + 1
    GROUP = 4
    BODY = 2 * GROUP
    TRIPS = T // BODY
    assert F == P and N == T * P and KEY0 + N <= 0x4000

    tables = [nc.dram_tensor(f"table{l}", [N + 1, TC], F32, kind="Internal").ap() for l in range(L)]

    with ExitStack() as ctx:
        def sb(name, shape, dt):
            return ctx.enter_context(nc.sbuf_tensor(name, shape, dt))

        def ps(name, shape, dt):
            return ctx.enter_context(nc.psum_tensor(name, shape, dt))

        def sem(name):
            return ctx.enter_context(nc.semaphore(name))

        xs = sb("xs", [P, T, XC], F32)
        ydense = sb("ydense", [P, T, F], F32)
        keys = ydense[:, :, :].rearrange("p t f -> p (t f)").bitcast(BF16)[:, 0:T * P].rearrange(
            "p (b i) -> p b i", i=P)
        slots = [sb(f"slots{b}", [P, CAP, TC], F32) for b in range(GROUP)]
        raw = [sb(f"raw{q}", [P, QW], I32) for q in range(QUARTERS)]
        exp_a = sb("exp_a", [P, CB, P], F32)
        exp_b = sb("exp_b", [P, CB, P], F32)
        halves = [e[:, :, :].rearrange("p c i -> p (c i)").bitcast(BF16) for e in (exp_a, exp_b)]
        signs = [halves[q // 2][:, (q % 2) * QW:(q % 2 + 1) * QW] for q in range(QUARTERS)]
        found = sb("found", [P, T, CAP + 8 + QUARTERS], F32)
        index = sb("index", [P, T, CAP], U32)
        absent = sb("absent", [P, T, CAP], F32)
        index_st = [sb(f"index_st{h}", [P, GROUP, CAP], U32) for h in range(2)]
        stage = [sb(f"stage{h}", [P, GROUP, XC], F32) for h in range(2)]
        w_agg = sb("w_agg", [P, L, F], F32)
        w_score = sb("w_score", [P, L, F], F32)
        a_sb = sb("a_sb", [P, 2 * L], F32)
        a_bc = sb("a_bc", [P, 2 * L, P], F32)
        wa = sb("wa", [P, 2 * L, F], F32)
        ident = sb("ident", [P, P], F32)
        ident_b = sb("ident_b", [P, P], BF16)
        ones = sb("ones", [P, P], F32)
        key_i = sb("key_i", [P, T], I32)
        key_f = sb("key_f", [P, T], F32)
        minus_half = sb("minus_half", [P, 1], F32)
        eps_c = sb("eps_c", [P, 1], F32)
        xsum = sb("xsum", [P, F], F32)
        prod = [sb(f"prod{h}", [P, 2, F], F32) for h in range(2)]
        cand = [sb(f"cand{i}", [P, QUARTERS * 8], F32) for i in range(3)]
        picked = sb("picked", [P, CAP + 8], F32)
        mean_row = sb("mean_row", [P, TC], F32)
        over = sb("over", [P, T], F32)
        degree = sb("degree", [P, T], F32)
        degree_m = sb("degree_m", [P, T], F32)
        k_col = sb("k_col", [T, 1], F32)
        k_row = sb("k_row", [1, T], F32)
        k_parts = sb("k_parts", [1, len(SLOT_GROUPS), T], F32)
        k_sum = sb("k_sum", [1, T], F32)
        dense_row = sb("dense_row", [1, T], F32)
        sparse_row = sb("sparse_row", [1, T], F32)
        count_row = sb("count_row", [1, T], F32)
        rev_i = sb("rev_i", [1, T], I32)
        rev_f = sb("rev_f", [1, T], F32)
        dense_key = [sb(f"dense_key{i}", [1, T], F32) for i in range(2)]
        dense_list = sb("dense_list", [1, T], F32)
        gather_k = sb("gather_k", [1, T], I32)
        sum_k = sb("sum_k", [1, T], I32)
        dense_ids = sb("dense_ids", [1, T], I32)
        dense_n = sb("dense_n", [1, 1], F32)
        dense_ni = sb("dense_ni", [1, 1], I32)
        z = [sb(f"z{i}", [P, CAP], F32) for i in range(2)]
        lk = [sb(f"lk{i}", [P, CAP], F32) for i in range(2)]
        neg_max = [sb(f"neg_max{i}", [P, 1], F32) for i in range(2)]
        prob = [sb(f"prob{i}", [P, CAP], F32) for i in range(2)]
        total = [sb(f"total{i}", [P, 1], F32) for i in range(2)]
        r_total = [sb(f"r_total{i}", [P, 2], F32) for i in range(2)]
        y_t = [sb(f"y_t{i}", [P, P], F32) for i in range(2)]
        neg_part = [sb(f"neg_part{i}", [P, F], F32) for i in range(2)]
        exp_part = [sb(f"exp_part{i}", [P, F], F32) for i in range(2)]
        act_out = [sb(f"act_out{i}", [P, F], F32) for i in range(2)]
        elu_out = [sb(f"elu_out{i}", [P, F], F32) for i in range(2)]
        res = [sb(f"res{i}", [P, F], F32) for i in range(2)]
        stats = [sb(f"stats{i}", [P, 6], F32) for i in range(2)]
        mean_var = [sb(f"mean_var{i}", [P, 2], F32) for i in range(2)]
        log_var = [sb(f"log_var{i}", [P, 1], F32) for i in range(2)]
        r_std = [sb(f"r_std{i}", [P, 1], F32) for i in range(2)]
        junk = sb("junk", [P, 2, F], F32)
        quarter_max = sb("quarter_max", [P, QUARTERS, P], F32)
        block_max = sb("block_max", [P, P], F32)
        d_sc = sb("d_sc", [P, 8], F32)
        d_diag = sb("d_diag", [P, 2, P], F32)
        d_rows = sb("d_rows", [P, 2, P], F32)
        a_s2 = sb("a_s2", [P, T], F32)
        d_y = sb("d_y", [P, F], F32)

        big = [ps(f"big{i}", [P, QW], F32) for i in range(2)]
        def region(k):
            return big[k // 4][:, (k % 4) * 512:(k % 4) * 512 + 512]
        yt_ps = [region(0)[:, 0:P], region(1)[:, 0:P]]
        o_ps = [region(2)[:, 0:P], region(3)[:, 0:P]]
        sum_ps = region(4)[:, 0:P]
        dense_ps = region(5)[:, 0:F + 1]
        misc_ps = region(6)
        misc2_ps = region(7)

        ld_x = sem("ld_x"); ld_w = sem("ld_w")
        raw_in = [sem(f"raw_in{q}") for q in range(QUARTERS)]
        sign_done = sem("sign_done")
        key_done = sem("key_done")
        max_done = sem("max_done")
        pick = sem("pick")
        prod_done = sem("prod_done")
        score_done = sem("score_done")
        t0_w = sem("t0_w")
        ready = sem("ready")
        dve = sem("dve")
        pe_step = sem("pe_step")
        act_step = sem("act_step")
        lists_done = sem("lists_done")
        stage_w = [sem(f"stage_w{h}") for h in range(2)]
        mean_w = sem("mean_w")
        idx_cp = sem("idx_cp")
        gat = [sem(f"gat{b}") for b in range(GROUP)]
        score = sem("score")
        prob_ok = sem("prob_ok")
        scaled = sem("scaled")
        r_ok = sem("r_ok")
        yt_ok = sem("yt_ok")
        yt_cp = sem("yt_cp")
        o_ok = sem("o_ok")
        elu_ok = sem("elu_ok")
        fin1 = sem("fin1")
        std_ok = sem("std_ok")
        norm_ok = sem("norm_ok")
        fin2 = sem("fin2")
        sum_ok = sem("sum_ok")
        xs_cp = sem("xs_cp")
        mean_ok = sem("mean_ok")
        sum_zero = sem("sum_zero")
        d_in = sem("d_in")
        d_free = sem("d_free")
        d_v = sem("d_v"); d_p = sem("d_p"); d_a = sem("d_a")
        d_e = sem("d_e"); d_m = sem("d_m"); d_q = sem("d_q")
        met = [sem("met_v"), sem("met_g")]

        def alone(eng):
            eng.sem_inc(met[eng is nc.gpsimd], 1)

        block = ctx.enter_context(nc.Block())

        def layer_fin1_steps(l):
            return {NONE: 3, RELU: 4, ELU: 5}[AFTER[l]]

        FIN1_AT = [0]
        for l in range(L):
            FIN1_AT.append(FIN1_AT[-1] + T * layer_fin1_steps(l))
        ELU_LAYERS = [l for l in range(L) if AFTER[l] == ELU]

        def elu_before(l):
            return T * sum(1 for e in ELU_LAYERS if e < l)

        table_rows = [t[0:N, :].rearrange("(t p) c -> p t c", p=P) for t in tables]
        out_rows = out.rearrange("(t p) f -> p t f", p=P)

        DV = 3 * QUARTERS + 9 + 3 * QUARTERS + 6

        @block.sync
        def _(sp):
            sp.dma_start(w_score[:, :, :], w_score_in).then_inc(ld_w, 16)
            sp.dma_start(a_sb[:, :], a_in).then_inc(ld_w, 16)
            sp.dma_start(xs[:, :, 1:F + 1], x_in.rearrange("(t p) f -> p t f", p=P)).then_inc(ld_x, 16)
            sp.dma_start(w_agg[:, :, :], w_agg_in).then_inc(ld_w, 16)
            for q in range(QUARTERS):
                sp.dma_start(raw[q][:, :], adj_in[0, q]).then_inc(raw_in[q], 16)
            with sp.Fori(1, T) as t:
                for q in range(QUARTERS):
                    sp.wait_ge(sign_done, 4 * t + (q - 3))
                    sp.dma_start(raw[q][:, :], adj_in[bass.ds(t, 1), q].rearrange("a p n -> (a p) n")).then_inc(raw_in[q], 16)
                sp.wait_ge(score_done, t + 2)
                sp.dma_start(table_rows[0][:, bass.ds(t - 1, 1), :], xs[:, bass.ds(t - 1, 1), 1:F + 2]).then_inc(t0_w, 16)
            sp.wait_ge(score_done, T + 2)
            sp.dma_start(table_rows[0][:, T - 1:T, :], xs[:, T - 1:T, 1:F + 2]).then_inc(stage_w[1], 16)
            sp.wait_ge(mean_ok, 1)
            sp.dma_start(tables[0][N:N + 1, :], mean_row[0:1, :]).then_inc(stage_w[0], 16)
            sp.wait_ge(lists_done, 1)
            for l in range(L):
                nd = sp.value_load(dense_ni[0:1, 0:1], min_val=0, max_val=T)
                with sp.If(nd > 0):
                    with sp.Fori(0, nd) as r:
                        t = sp.value_load(dense_ids[0:1, bass.ds(r, 1)], min_val=0, max_val=T - 1)
                        sp.wait_ge(d_free, r + nd * l + 1)
                        for q in range(QUARTERS):
                            sp.dma_start(raw[q][:, :], adj_in[bass.ds(t, 1), q].rearrange("a p n -> (a p) n")).then_inc(d_in, 16)
                with sp.Fori(0, TRIPS) as g:
                    for h in range(2):
                        n = BODY * l * TRIPS + BODY * g + GROUP * (h + 1)
                        sp.wait_ge(fin2, n)
                        if l < L - 1:
                            dst = table_rows[l + 1][:, bass.ds(BODY * g + GROUP * h, GROUP), :]
                            sp.dma_start(dst, stage[h][:, :, 1:F + 2]).then_inc(stage_w[h], 16)
                        else:
                            dst = out_rows[:, bass.ds(BODY * g + GROUP * h, GROUP), :]
                            sp.dma_start(dst, stage[h][:, :, 1:F + 1]).then_inc(stage_w[h], 16)
                if l < L - 1:
                    sp.wait_ge(mean_ok, l + 2)
                    sp.dma_start(tables[l + 1][N:N + 1, :], mean_row[0:1, :]).then_inc(mean_w, 16)
            for h in range(2):
                sp.wait_ge(stage_w[h], 16 * (L * TRIPS + 1))
            sp.wait_ge(t0_w, 16 * (T - 1))
            sp.wait_ge(mean_w, 16 * (L - 1))

        @block.gpsimd
        def _(pool):
            pool.memset(ones[:, :], 1.0).then_inc(ready, 1)
            pool.iota(key_i[:, :], pattern=[[P, T]], base=KEY0, channel_multiplier=1).then_inc(ready, 1)
            pool.iota(rev_i[:, :], pattern=[[-1, T]], base=T, channel_multiplier=0).then_inc(ready, 1)
            pool.wait_ge(ready, 1)
            pool.affine_select(out=ident[:, :], in_=ones[:, :], compare_op=ALU.is_equal, fill=0.0, base=0,
                               pattern=[[-1, P]], channel_multiplier=1).then_inc(ready, 1)
            pool.wait_ge(ld_x, 16)
            pool.wait_ge(act_step, 1)
            with pool.Fori(0, T // 2) as t2:
                for h in range(2):
                    t = 2 * t2 + h
                    pool.wait_ge(score_done, t + 1)
                    pool.tensor_tensor(prod[h][:, 0, :], xs[:, bass.ds(t, 1), 1:F + 1].rearrange("p a f -> p (a f)"),
                                       wa[:, 1, :], ALU.mult)
                    pool.tensor_tensor(prod[h][:, 1, :], xs[:, bass.ds(t, 1), 1:F + 1].rearrange("p a f -> p (a f)"),
                                       wa[:, 0, :], ALU.mult).then_inc(prod_done, 1)
            for b in range(GROUP):
                pool.memset(slots[b][:, :, :], 0.0).then_inc(ready, 1)
            pool.wait_ge(ready, 4 + GROUP)
            pool.wait_ge(lists_done, 1)
            pool.wait_ge(t0_w, 16 * (T - 1))
            for l in range(L):
                if l > 0:
                    pool.wait_ge(mean_w, 16 * l)
                for h in range(2):
                    pool.wait_ge(stage_w[h], 16 * (l * TRIPS + 1))
                with pool.Fori(0, TRIPS) as g:
                    for h in range(2):
                        i = 2 * TRIPS * l + 2 * g + h
                        pool.tensor_copy(index_st[h][:, :, :], index[:, bass.ds(BODY * g + GROUP * h, GROUP), :]).then_inc(idx_cp, 1)
                        pool.wait_ge(idx_cp, i + 1)
                        for b in range(GROUP):
                            n = T * l + BODY * g + GROUP * h + b
                            k = pool.value_load(gather_k[0:1, bass.ds(BODY * g + GROUP * h + b, 1)], min_val=1, max_val=CAP)
                            pool.wait_ge(yt_ok, n + 1)
                            alone(pool)

                            def gather(first, count):
                                for s in range(first, first + count):
                                    pool.indirect_dma_start(slots[b][:, s, :], None, tables[l],
                                                            bass.IndirectOffsetOnAxis(index_st[h][:, b, s:s + 1], 0),
                                                            bounds_check=N, oob_is_err=False).then_inc(gat[b], 16)

                            gather(*SLOT_GROUPS[0])
                            for first, count in SLOT_GROUPS[1:]:
                                with pool.If(k > first):
                                    gather(first, count)

        @block.scalar
        def _(act):
            act.preload_act_table_set("natural_log_exp_and_others")
            act.sem_inc(xs_cp, 1)
            act.wait_ge(pe_step, 1)
            act.activation(wa[:, 0:4, :], misc_ps.rearrange("p (a f) -> p a f", f=F), ACT.Copy)
            act.activation(wa[:, 4:8, :], misc2_ps.rearrange("p (a f) -> p a f", f=F), ACT.Copy).then_inc(act_step, 1)
            act.wait_ge(dve, 1)
            with act.Fori(0, T) as t:
                for q in range(QUARTERS):
                    act.wait_ge(raw_in[q], 16 * t + 16)
                    act.wait_ge(key_done, 4 * t + (q + 1))
                    act.activation(signs[q], raw[q][:, :], ACT.Sign, bias=minus_half[:, 0:1]).then_inc(sign_done, 1)
            act.wait_ge(pe_step, 2)
            act.activation(mean_row[:, 0:F], sum_ps, ACT.Copy, scale=1.0 / N).then_inc(mean_ok, 1)

            for l in range(L):
                elu = AFTER[l] == ELU
                if l == 0:
                    act.wait_ge(lists_done, 1)
                nd = act.value_load(dense_ni[0:1, 0:1], min_val=0, max_val=T)
                with act.If(nd > 0):
                    with act.Fori(0, nd) as r:
                        R = r + nd * l
                        act.wait_ge(d_p, 3 * R + 2)
                        act.activation(d_rows[:, :, :], misc_ps[:, 0:2 * P].rearrange("p (a i) -> p a i", a=2), ACT.Copy).then_inc(d_a, 1)
                        for q in range(QUARTERS):
                            act.wait_ge(d_e, QUARTERS * R + (q + 1))
                            for c in range(CB):
                                b = QUARTERS * c + q
                                act.activation(exp_a[:, c, :], exp_a[:, c, :], ACT.Exp, bias=xs[:, b, F + 1:F + 2])
                                last = act.activation(exp_b[:, c, :], exp_b[:, c, :], ACT.Exp, bias=a_s2[:, b:b + 1])
                            last.then_inc(d_m, 1)

                def finish(n, u, g):
                    i = u % 2
                    act.wait_ge(fin1, FIN1_AT[l] + layer_fin1_steps(l) * (BODY * g + u + 1))
                    act.activation(log_var[i][:, :], mean_var[i][:, 1:2], ACT.Ln, bias=eps_c[:, 0:1]).then_inc(std_ok, 1)
                    act.wait_ge(std_ok, 2 * n + 1)
                    act.activation(r_std[i][:, :], log_var[i][:, :], ACT.Exp, scale=-0.5).then_inc(std_ok, 1)

                def elu_part(n, u, g):
                    i = u % 2
                    e = elu_before(l) + BODY * g + u
                    act.wait_ge(o_ok, n + 3)
                    act.wait_ge(r_ok, n + 1)
                    act.activation(neg_part[i][:, :], o_ps[i], ACT.Relu, scale=r_total[i][:, 1:2]).then_inc(elu_ok, 1)
                    act.wait_ge(elu_ok, 2 * e + 1)
                    act.activation(exp_part[i][:, :], neg_part[i][:, :], ACT.Exp, scale=-1.0).then_inc(elu_ok, 1)

                with act.Fori(0, TRIPS) as g:
                    base = T * l + BODY * g
                    for u in range(BODY + 2):
                        if u < BODY:
                            i = u % 2
                            act.wait_ge(score, 3 * (base + u) + 3)
                            act.activation(prob[i][:, :], lk[i][:, :], ACT.Exp, bias=neg_max[i][:, 0:1],
                                           accum_out=total[i][:, 0:1]).then_inc(prob_ok, 1)
                        if u >= 2:
                            finish(base + u - 2, u - 2, g)
                        if 1 <= u < BODY + 1:
                            j = u - 1
                            act.wait_ge(yt_ok, GROUP + base + j + 1)
                            act.wait_ge(o_ok, base + j + 1)
                            act.activation(y_t[j % 2][:, :], yt_ps[j % 2], ACT.Copy).then_inc(yt_cp, 1)
                            if elu:
                                elu_part(base + j, j, g)
                    if l < L - 1:
                        act.wait_ge(fin2, base + BODY)
                        for h in range(2):
                            act.activation(xs[:, bass.ds(BODY * g + GROUP * h, GROUP), 1:XC], stage[h][:, :, 1:XC],
                                           ACT.Copy).then_inc(xs_cp, 1)
                if l < L - 1:
                    act.wait_ge(sum_ok, T * (l + 1) + 1)
                    act.wait_ge(mean_w, 16 * l) if l > 0 else act.wait_ge(stage_w[0], 16)
                    act.activation(mean_row[:, 0:F], sum_ps, ACT.Copy, scale=1.0 / N).then_inc(mean_ok, 1)

        @block.tensor
        def _(pe):
            pe.wait_ge(dve, 2)
            pe.wait_ge(ld_w, 48)
            for j in range(2 * L):
                where = (misc_ps if j < 4 else misc2_ps)[:, (j % 4) * F:(j % 4 + 1) * F]
                mm = pe.matmul(where, a_bc[:, j, :], w_score[:, j // 2, :], start=True, stop=True)
            mm.then_inc(pe_step, 1)
            pe.sem_inc(key_done, 4)
            pe.sem_inc(yt_ok, GROUP)
            pe.sem_inc(o_ok, 2)
            pe.sem_inc(sum_ok, 1)
            pe.wait_ge(act_step, 1)
            pe.wait_ge(dve, 4)
            with pe.Fori(0, T) as t:
                for q in range(QUARTERS):
                    pe.wait_ge(sign_done, 4 * t + (q + 1))
                    pe.wait_ge(max_done, 4 * t + (q + 1))
                    for c in range(CB):
                        mm = pe.matmul(big[q % 2][:, c * P:(c + 1) * P], signs[q][:, c * P:(c + 1) * P],
                                       keys[:, QUARTERS * c + q, :], start=True, stop=True)
                    mm.then_inc(key_done, 1)
            pe.wait_ge(max_done, 4 * T + 2)
            pe.wait_ge(dve, 5)
            pe.matmul(sum_ps, ones[:, :], xsum[:, :], start=True, stop=True).then_inc(pe_step, 1)
            pe.wait_ge(dve, 10)
            pe.transpose(misc_ps[0:T, 0:P], degree_m[:, :], ident[:, :]).then_inc(pe_step, 1)
            pe.wait_ge(dve, 11)
            pe.matmul(misc2_ps[0:1, 0:T], k_col[:, :], ident[0:T, 0:T], start=True, stop=True).then_inc(pe_step, 1)
            pe.wait_ge(dve, 13)
            pe.matmul(misc_ps[:, 256:256 + T], ones[0:1, :], dense_row[0:1, :], start=True, stop=True).then_inc(pe_step, 1)
            pe.wait_ge(lists_done, 1)
            for l in range(L):
                nd = pe.value_load(dense_ni[0:1, 0:1], min_val=0, max_val=T)
                with pe.If(nd > 0):
                    with pe.Fori(0, nd) as r:
                        R = r + nd * l
                        D = DV * R
                        pe.wait_ge(d_v, D + 3 * QUARTERS + 1)
                        pe.transpose(misc2_ps[:, 0:P], block_max[:, :], ident[:, :]).then_inc(d_p, 1)
                        pe.wait_ge(d_v, D + 3 * QUARTERS + 8)
                        for k in range(2):
                            mm = pe.matmul(misc_ps[:, k * P:(k + 1) * P], ones[:, :], d_diag[:, k, :], start=True, stop=True)
                        mm.then_inc(d_p, 1)
                        for q in range(QUARTERS):
                            pe.wait_ge(d_v, D + 3 * QUARTERS + 9 + 3 * (q + 1))
                            for c in range(CB):
                                b = QUARTERS * c + q
                                mm = pe.matmul(dense_ps, exp_a[:, c, :], xs[:, b, 0:F + 1], start=(b == 0),
                                               stop=(q == QUARTERS - 1 and c == CB - 1))
                            mm.then_inc(d_q, 1)
                        pe.wait_ge(d_v, D + DV - 1)
                        pe.transpose(misc2_ps[:, 0:P], d_y[:, :], ident[:, :]).then_inc(d_p, 1)
                if l < L - 1:
                    pe.wait_ge(sum_zero, l + 1)

                def times_w(n, u):
                    pe.wait_ge(yt_cp, n + 1)
                    pe.wait_ge(norm_ok, n + 1)
                    pe.matmul(o_ps[u % 2], y_t[u % 2][:, :], w_agg[:, l, :], start=True, stop=True).then_inc(o_ok, 1)

                def add_rows(n, u):
                    pe.wait_ge(norm_ok, n + 3)
                    pe.matmul(sum_ps, ones[:, :], stage[u // GROUP][:, u % GROUP, 1:F + 1], start=False, stop=False,
                              skip_group_check=True).then_inc(sum_ok, 1)

                def add_slots(n, u, k, t):
                    b, i = u % GROUP, u % 2

                    def add(first, count, start=False):
                        for s in range(first, first + count):
                            mm = pe.matmul(yt_ps[i], slots[b][:, s, 0:F], ident[:, :], start=start, stop=False,
                                           skip_group_check=True)
                        return mm

                    pe.wait_ge(scaled, n + 1)
                    with pe.If(k > 1):
                        add(0, 1, start=True)
                        for first, count in SLOT_GROUPS[:1:-1]:
                            with pe.If(k > first):
                                add(first, count)
                        add(1, 1).then_inc(yt_ok, 1)
                    with pe.Else():
                        with pe.If(k > 0):
                            add(0, 1, start=True).then_inc(yt_ok, 1)
                        with pe.Else():
                            pe.matmul(yt_ps[i], ident[:, :], ydense[:, bass.ds(t, 1), :].rearrange("p a i -> p (a i)"),
                                      start=True, stop=False, skip_group_check=True).then_inc(yt_ok, 1)

                with pe.Fori(0, TRIPS) as g:
                    base = T * l + BODY * g
                    for u in range(BODY + 3):
                        if u < BODY:
                            k = pe.value_load(sum_k[0:1, bass.ds(BODY * g + u, 1)], min_val=0, max_val=CAP)
                        if 1 <= u < BODY + 1:
                            times_w(base + u - 1, u - 1)
                        if u < BODY:
                            add_slots(base + u, u, k, BODY * g + u)
                        if l < L - 1 and u >= 3:
                            add_rows(base + u - 3, u - 3)

        @block.vector
        def _(d):
            d.memset(minus_half[:, :], -0.5)
            d.memset(eps_c[:, :], EPS)
            d.memset(mean_row[:, F:TC], 0.0)
            d.memset(key_f[:, :], 0.0)
            d.memset(xs[:, :, 0:1], 1.0).then_inc(dve, 1)
            d.sem_inc(max_done, 2)
            d.sem_inc(pick, 1)
            d.sem_inc(score_done, 2)
            d.sem_inc(norm_ok, 2)
            d.sem_inc(d_free, 1)
            d.wait_ge(ready, 4)
            d.wait_ge(ld_w, 48)
            for j in range(2 * L):
                last = d.tensor_scalar(a_bc[:, j, :], ones[:, :], a_sb[:, j:j + 1], None, ALU.mult)
            last.then_inc(dve, 1)
            d.wait_ge(dve, 2)
            d.tensor_copy(key_f[:, :].bitcast(U16).rearrange("p (t two) -> p t two", two=2)[:, :, 1], key_i[:, :])
            d.tensor_copy(ident_b[:, :], ident[:, :]).then_inc(dve, 1)
            d.wait_ge(dve, 3)
            d.tensor_tensor(keys, ident_b[:, :].unsqueeze(1).to_broadcast([P, T, P]),
                            key_f[:, :].unsqueeze(2).to_broadcast([P, T, P]), ALU.mult).then_inc(dve, 1)
            d.wait_ge(ld_x, 16)
            d.tensor_reduce(xsum[:, :], xs[:, :, 1:F + 1].rearrange("p t f -> p f t"), AX.X, ALU.add).then_inc(dve, 1)
            with d.Fori(0, T // 2) as t2:
                for h in range(2):
                    t = 2 * t2 + h
                    base = 7 * t
                    for q in range(QUARTERS):
                        d.wait_ge(key_done, 4 * t + (QUARTERS + q + 1))
                        if q == 0:
                            d.wait_ge(pick, base + 1)
                        alone(d)
                        d.max(out=cand[0][:, 8 * q:8 * q + 8], in_=big[q % 2][:, :]).then_inc(max_done, 1)
                    d.wait_ge(prod_done, t + 1)
                    d.tensor_reduce(xs[:, bass.ds(t, 1), F + 1:F + 3].rearrange("p a s -> p (a s)"), prod[h][:, :, :],
                                    AX.X, ALU.add).then_inc(score_done, 1)
                    d.wait_ge(max_done, 4 * t + 6)
                    alone(d)
                    d.max(out=picked[:, 0:8], in_=cand[0][:, :]).then_inc(pick, 1)
                    d.wait_ge(pick, base + 2)
                    alone(d)
                    d.match_replace(out=cand[1][:, :], in_to_replace=picked[:, 0:8], in_values=cand[0][:, :],
                                    imm_value=-1.0).then_inc(pick, 1)
                    d.wait_ge(pick, base + 3)
                    alone(d)
                    d.max(out=picked[:, 8:16], in_=cand[1][:, :]).then_inc(pick, 1)
                    d.wait_ge(pick, base + 4)
                    alone(d)
                    d.match_replace(out=cand[2][:, :], in_to_replace=picked[:, 8:16], in_values=cand[1][:, :],
                                    imm_value=-1.0).then_inc(pick, 1)
                    d.wait_ge(pick, base + 5)
                    alone(d)
                    d.max(out=picked[:, 16:24], in_=cand[2][:, :]).then_inc(pick, 1)
                    d.wait_ge(pick, base + 6)
                    d.tensor_copy(found[:, bass.ds(t, 1), 0:CAP + 8].rearrange("p a k -> p (a k)"), picked[:, :]).then_inc(pick, 1)
                    d.tensor_copy(found[:, bass.ds(t, 1), CAP + 8:CAP + 8 + QUARTERS].rearrange("p a k -> p (a k)"),
                                  cand[0][:, 7::8]).then_inc(pick, 1)
            d.wait_ge(pick, 7 * T + 1)
            step = [5]

            def then(ins):
                step[0] += 1
                ins.then_inc(dve, 1)

            top = found[:, :, 0:CAP]
            top_u = found[:, :, :].bitcast(U16).rearrange("p t (k two) -> p t k two", two=2)[:, :, 0:CAP, 1]
            flag = absent[:, :, :]
            then(d.tensor_scalar(flag, top, 0.0, None, ALU.is_gt))
            then(d.tensor_reduce(over[:, :], found[:, :, CAP:CAP + 8 + QUARTERS], AX.X, ALU.max))
            d.wait_ge(dve, 6)
            then(d.tensor_reduce(degree[:, :], flag, AX.X, ALU.add))
            d.wait_ge(dve, 7)
            then(d.tensor_scalar(over[:, :], over[:, :], 0.0, DENSE_MARK, ALU.is_gt, ALU.mult))
            d.wait_ge(dve, 9)
            then(d.tensor_tensor(degree_m[:, :], degree[:, :], over[:, :], ALU.add))
            d.wait_ge(pe_step, 3)
            then(d.tensor_reduce(k_col[:, :], misc_ps[0:T, 0:P], AX.X, ALU.max))
            d.wait_ge(pe_step, 4)
            then(d.tensor_copy(k_row[:, :], misc2_ps[0:1, 0:T]))
            d.wait_ge(dve, 12)
            then(d.tensor_scalar(dense_row[:, :], k_row[:, :], DENSE_MARK / 2, None, ALU.is_gt))
            for j, (first, count) in enumerate(SLOT_GROUPS):
                d.tensor_scalar(k_parts[:, j, :], k_row[:, :], float(first) if j else -1.0, float(count), ALU.is_gt, ALU.mult)
            then(d.tensor_copy(rev_f[:, :], rev_i[:, :]))
            d.wait_ge(dve, 14)
            then(d.tensor_reduce(k_sum[:, :], k_parts[:, :, :].rearrange("o j t -> o t j"), AX.X, ALU.add))
            then(d.tensor_scalar(sparse_row[:, :], dense_row[:, :], -1.0, 1.0, ALU.mult, ALU.add))
            then(d.tensor_reduce(dense_n[:, :], dense_row[:, :], AX.X, ALU.add))
            then(d.tensor_tensor(dense_key[0][:, :], dense_row[:, :], rev_f[:, :], ALU.mult))
            d.wait_ge(dve, 18)
            then(d.tensor_tensor(count_row[:, :], k_sum[:, :], sparse_row[:, :], ALU.mult))
            then(d.tensor_copy(dense_ni[:, :], dense_n[:, :]))
            d.wait_ge(dve, 19)
            then(d.tensor_copy(sum_k[:, :], count_row[:, :]))
            then(d.tensor_scalar(gather_k[:, :], count_row[:, :], 1.0, None, ALU.max))
            for j in range(T // 8):
                d.wait_ge(dve, step[0])
                then(d.max(out=dense_list[:, 8 * j:8 * j + 8], in_=dense_key[j % 2][:, :]))
                d.wait_ge(dve, step[0])
                then(d.match_replace(out=dense_key[(j + 1) % 2][:, :], in_to_replace=dense_list[:, 8 * j:8 * j + 8],
                                     in_values=dense_key[j % 2][:, :], imm_value=0.0))
            d.wait_ge(dve, step[0])
            then(d.tensor_scalar(dense_ids[:, :], dense_list[:, :], -1.0, float(T), ALU.mult, ALU.add))
            idx_f = exp_a[:, :, :].rearrange("p c i -> p (c i)")[:, 0:T * CAP].rearrange("p (t k) -> p t k", k=CAP)
            then(d.tensor_scalar(idx_f, top_u, float(KEY0), float(N), ALU.subtract, ALU.min))
            d.wait_ge(pe_step, 5)
            d.wait_ge(dve, step[0])
            dense_bc = misc_ps[:, 256:256 + T].unsqueeze(2).to_broadcast([P, T, CAP])
            then(d.scalar_tensor_tensor(out=idx_f, in0=dense_bc, scalar=float(N), in1=idx_f, op0=ALU.mult, op1=ALU.max))
            d.wait_ge(dve, step[0])
            then(d.tensor_copy(index[:, :, :], idx_f))
            then(d.tensor_scalar(absent[:, :, :], idx_f, float(N) - 0.5, -BIG, ALU.is_gt, ALU.mult))
            d.wait_ge(dve, step[0])
            then(d.memset(absent[:, :, 0:1], 0.0))
            d.wait_ge(dve, step[0])
            d.sem_inc(lists_done, 1)

            gathered = [d.alloc_register(f"gathered{b}") for b in range(GROUP)]
            for b in range(GROUP):
                d.reg_mov(gathered[b], 0)

            for l in range(L):
                alpha = SLOPES[l]
                kind = AFTER[l]
                d.wait_ge(mean_ok, l + 1)
                if l < L - 1:
                    d.memset(sum_ps, 0.0).then_inc(sum_zero, 1)
                d.wait_ge(xs_cp, 2 * TRIPS * l + 1)
                nd = d.value_load(dense_ni[0:1, 0:1], min_val=0, max_val=T)
                with d.If(nd > 0):
                    with d.Fori(0, nd) as r:
                        R = r + nd * l
                        D = DV * R
                        t = d.value_load(dense_ids[0:1, bass.ds(r, 1)], min_val=0, max_val=T - 1)
                        k = 0

                        def dstep(ins):
                            nonlocal k
                            k += 1
                            ins.then_inc(d_v, 1)

                        d.wait_ge(d_in, 16 * QUARTERS * R + 16 * QUARTERS)
                        s2 = xs[:, :, F + 1:F + 2]
                        masked = [raw[q][:, :].bitcast(F32).rearrange("p (c i) -> p c i", i=P) for q in range(QUARTERS)]
                        for q in range(QUARTERS):
                            dstep(d.tensor_scalar(masked[q], raw[q][:, :].rearrange("p (c i) -> p c i", i=P), 0.0, -BIG,
                                                  ALU.is_le, ALU.mult))
                            d.wait_ge(d_v, D + k)
                            dstep(d.tensor_tensor(exp_a[:, :, :], masked[q], s2[:, q::QUARTERS, :].to_broadcast([P, CB, P]), ALU.add))
                            d.wait_ge(d_v, D + k)
                            dstep(d.tensor_reduce(quarter_max[:, q, :], exp_a[:, :, :].rearrange("p c i -> p i c"), AX.X, ALU.max))
                            d.wait_ge(d_v, D + k)
                        dstep(d.tensor_reduce(block_max[:, :], quarter_max[:, :, :].rearrange("p q i -> p i q"), AX.X, ALU.max))
                        d.wait_ge(d_p, 3 * R + 1)
                        dstep(d.tensor_reduce(d_sc[:, 0:1], misc2_ps[:, 0:P], AX.X, ALU.max))
                        s1 = xs[:, bass.ds(t, 1), F + 2:F + 3].rearrange("p a s -> p (a s)")
                        d.wait_ge(d_v, D + k)
                        dstep(d.tensor_tensor(d_sc[:, 1:2], d_sc[:, 0:1], s1, ALU.add))
                        d.wait_ge(d_v, D + k)
                        dstep(d.scalar_tensor_tensor(out=d_sc[:, 2:3], in0=d_sc[:, 1:2], scalar=alpha, in1=d_sc[:, 1:2],
                                                     op0=ALU.mult, op1=ALU.max))
                        d.wait_ge(d_v, D + k)
                        dstep(d.tensor_tensor(d_sc[:, 3:4], s1, d_sc[:, 2:3], ALU.subtract))
                        dstep(d.scalar_tensor_tensor(out=d_sc[:, 4:5], in0=s1, scalar=alpha, in1=d_sc[:, 2:3],
                                                     op0=ALU.mult, op1=ALU.subtract))
                        d.wait_ge(d_v, D + k)
                        dstep(d.tensor_scalar(d_diag[:, 0, :], ident[:, :], d_sc[:, 3:4], None, ALU.mult))
                        dstep(d.tensor_scalar(d_diag[:, 1, :], ident[:, :], d_sc[:, 4:5], None, ALU.mult))
                        assert k == 3 * QUARTERS + 8
                        dstep(d.tensor_scalar(a_s2[:, :], s2.rearrange("p t s -> p (t s)"), alpha, None, ALU.mult))
                        d.wait_ge(d_a, R + 1)
                        for q in range(QUARTERS):
                            if q > 0:
                                d.wait_ge(d_q, QUARTERS * R + q)
                            d.wait_ge(d_v, D + k)
                            for buf, j in ((exp_a, 0), (exp_b, 1)):
                                last = d.tensor_tensor(buf[:, :, :], masked[q],
                                                       d_rows[:, j, :].unsqueeze(1).to_broadcast([P, CB, P]), ALU.add)
                                dstep(last)
                            d.wait_ge(d_v, D + k)
                            d.sem_inc(d_e, 1)
                            d.wait_ge(d_m, QUARTERS * R + (q + 1))
                            dstep(d.tensor_tensor(exp_a[:, :, :], exp_a[:, :, :], exp_b[:, :, :], ALU.max))
                        d.wait_ge(d_q, QUARTERS * R + QUARTERS)
                        dstep(d.tensor_scalar(d_sc[:, 5:6], dense_ps[:, 0:1], 0.0, None, ALU.is_le))
                        d.wait_ge(d_v, D + k)
                        dstep(d.tensor_tensor(d_sc[:, 6:7], dense_ps[:, 0:1], d_sc[:, 5:6], ALU.add))
                        dstep(d.scalar_tensor_tensor(out=d_y[:, :], in0=mean_row[:, 0:F], scalar=d_sc[:, 5:6],
                                                     in1=dense_ps[:, 1:F + 1], op0=ALU.mult, op1=ALU.add))
                        d.wait_ge(d_v, D + k)
                        dstep(d.reciprocal(d_sc[:, 7:8], d_sc[:, 6:7]))
                        d.wait_ge(d_v, D + k)
                        dstep(d.tensor_scalar(d_y[:, :], d_y[:, :], d_sc[:, 7:8], None, ALU.mult))
                        d.wait_ge(d_p, 3 * R + 3)
                        dstep(d.tensor_copy(ydense[:, bass.ds(t, 1), :].rearrange("p a i -> p (a i)"), misc2_ps[:, 0:P]))
                        assert k == DV, (k, DV)
                        d.wait_ge(d_v, D + k)
                        d.sem_inc(d_free, 1)

                def scores(n, u, g):
                    b, i = u % GROUP, u % 2
                    t = BODY * g + u
                    k = d.value_load(gather_k[0:1, bass.ds(t, 1)], min_val=1, max_val=CAP)
                    d.reg_add(gathered[b], gathered[b], 16 * k)
                    d.wait_ge(gat[b], d.snap(gathered[b]))
                    d.scalar_tensor_tensor(
                        out=z[i][:, :], in0=slots[b][:, :, F:F + 1].rearrange("p k c -> p (k c)"),
                        scalar=xs[:, bass.ds(t, 1), F + 2:F + 3].rearrange("p a s -> p (a s)"),
                        in1=absent[:, bass.ds(t, 1), :].rearrange("p a k -> p (a k)"), op0=ALU.add, op1=ALU.add).then_inc(score, 1)
                    d.wait_ge(score, 3 * n + 1)
                    d.scalar_tensor_tensor(out=lk[i][:, :], in0=z[i][:, :], scalar=alpha, in1=z[i][:, :],
                                           op0=ALU.mult, op1=ALU.max).then_inc(score, 1)
                    d.wait_ge(score, 3 * n + 2)
                    d.tensor_reduce(neg_max[i][:, :], lk[i][:, :], AX.X, ALU.max, negate=True).then_inc(score, 1)
                    return k

                def scale(n, u, k):
                    b, i = u % GROUP, u % 2
                    d.wait_ge(prob_ok, n + 1)
                    recip = d.reciprocal(r_total[i][:, 0:1], total[i][:, :])
                    if kind != ELU:
                        recip.then_inc(r_ok, 1)

                    def some(first, count):
                        view = slots[b][:, first:first + count, 0:F]
                        return d.tensor_tensor(view, view, prob[i][:, first:first + count].unsqueeze(2).to_broadcast([P, count, F]),
                                               ALU.mult)

                    for first, count in SLOT_GROUPS[:0:-1]:
                        with d.If(k > first):
                            some(first, count)
                    some(*SLOT_GROUPS[0]).then_inc(scaled, 1)
                    if kind == ELU:
                        d.wait_ge(scaled, n + 1)
                        d.tensor_scalar(r_total[i][:, 1:2], r_total[i][:, 0:1], -1.0, None, ALU.mult).then_inc(r_ok, 1)

                def finish1(n, u, g):
                    i = u % 2
                    t = BODY * g + u
                    x = xs[:, bass.ds(t, 1), 1:F + 1].rearrange("p a f -> p (a f)")
                    at = FIN1_AT[l] + layer_fin1_steps(l) * t
                    j = 0

                    def chain(ins, wait=True):
                        nonlocal j
                        ins.then_inc(fin1, 1)
                        j += 1
                        if wait:
                            d.wait_ge(fin1, at + j)

                    d.wait_ge(o_ok, n + 3)
                    d.wait_ge(r_ok, n + 1)
                    rt = r_total[i][:, 0:1]
                    if kind == NONE:
                        chain(d.scalar_tensor_tensor(out=res[i][:, :], in0=o_ps[i], scalar=rt, in1=x, op0=ALU.mult, op1=ALU.add))
                    elif kind == RELU:
                        chain(d.tensor_scalar(act_out[i][:, :], o_ps[i], rt, 0.0, ALU.mult, ALU.max))
                        chain(d.tensor_tensor(res[i][:, :], act_out[i][:, :], x, ALU.add))
                    else:
                        d.wait_ge(elu_ok, 2 * (elu_before(l) + t) + 1)
                        chain(d.tensor_scalar(act_out[i][:, :], o_ps[i], rt, None, ALU.mult))
                        d.wait_ge(elu_ok, 2 * (elu_before(l) + t) + 2)
                        chain(d.scalar_tensor_tensor(out=elu_out[i][:, :], in0=exp_part[i][:, :], scalar=-1.0,
                                                     in1=act_out[i][:, :], op0=ALU.add, op1=ALU.max))
                        chain(d.tensor_tensor(res[i][:, :], elu_out[i][:, :], x, ALU.add))
                    chain(d.bn_stats(stats[i][:, :], res[i][:, :]))
                    alone(d)
                    chain(d.bn_aggr(mean_var[i][:, :], stats[i][:, :]), wait=False)

                def finish2(n, u, g):
                    i, h, j = u % 2, u // GROUP, u % GROUP
                    m = TRIPS * l + g
                    d.wait_ge(std_ok, 2 * n + 2)
                    if j == 0:
                        d.wait_ge(stage_w[h], 16 * m + 16)
                        if h == 0:
                            before = m if l < L - 1 else TRIPS * l
                            d.wait_ge(xs_cp, 2 * before + 1)
                            d.wait_ge(sum_ok, BODY * before + 1)
                    xn = stage[h][:, j, 1:F + 1]
                    d.tensor_scalar(xn, res[i][:, :], mean_var[i][:, 0:1], r_std[i][:, 0:1], ALU.subtract, ALU.mult).then_inc(norm_ok, 1)
                    d.wait_ge(norm_ok, n + 3)
                    if l < L - 1:
                        for s, w in ((0, 2 * (l + 1) + 1), (1, 2 * (l + 1))):
                            last = d.tensor_tensor_reduce(out=junk[:, s, :], in0=xn, in1=wa[:, w, :], scale=1.0, scalar=0.0,
                                                          op0=ALU.mult, op1=ALU.add, accum_out=stage[h][:, j, F + 1 + s:F + 2 + s])
                        last.then_inc(fin2, 1)
                    else:
                        d.sem_inc(fin2, 1)

                with d.Fori(0, TRIPS) as g:
                    base = T * l + BODY * g
                    ks = {0: scores(base, 0, g)}
                    for u in range(BODY + 2):
                        if u + 1 < BODY:
                            ks[u + 1] = scores(base + u + 1, u + 1, g)
                        if u < BODY:
                            scale(base + u, u, ks[u])
                        if 1 <= u < BODY + 1:
                            finish1(base + u - 1, u - 1, g)
                        if 2 <= u < BODY + 2:
                            finish2(base + u - 2, u - 2, g)


def kernel(x, adj, L0_gnn_W, L0_gnn_a, L1_gnn_W, L1_gnn_a, L2_gnn_W, L2_gnn_a, L3_gnn_W, L3_gnn_a):
    import numpy as np
    import concourse.bacc as bacc
    from concourse import mybir as mb
    from concourse.bass_utils import run_bass_kernel_spmd

    x = np.ascontiguousarray(x)
    N, F = x.shape
    T = N // P
    adj = np.asarray(adj).reshape(T, P, T // QUARTERS, QUARTERS, P).transpose(0, 3, 4, 2, 1)
    adj = np.ascontiguousarray(adj).reshape(T, QUARTERS, P, (T // QUARTERS) * P)
    W = [np.asarray(w) for w in (L0_gnn_W, L1_gnn_W, L2_gnn_W, L3_gnn_W)]
    A = [np.asarray(a) for a in (L0_gnn_a, L1_gnn_a, L2_gnn_a, L3_gnn_a)]
    w_agg = np.ascontiguousarray(np.stack([W[0], W[1], W[2], W[3].T], axis=1))
    w_score = np.ascontiguousarray(np.stack([W[0].T, W[1].T, W[2].T, W[3]], axis=1))
    a = np.ascontiguousarray(np.stack([v for m in A for v in (m[:F, 0], m[F:, 0])], axis=1))

    nc = bacc.Bacc("TRN2", target_bir_lowering=False, num_devices=1)
    arrays, aps = {}, []
    for name, v in (("x", x), ("adj", adj), ("w_agg", w_agg), ("w_score", w_score), ("a", a)):
        arrays[f"in_{name}"] = v
        aps.append(nc.dram_tensor(f"in_{name}", v.shape, mb.dt.from_np(v.dtype), kind="ExternalInput").ap())
    out = nc.dram_tensor("out", (N, F), mb.dt.float32, kind="ExternalOutput").ap()
    gat_layers(nc, *aps, out)
    r = run_bass_kernel_spmd(nc, [arrays], core_ids=[0])
    return r.results[0]["out"]
```
